# Optimizing a Trainium2 kernel written in Bass

```python
import numpy as np
import jax
import jax.numpy as jnp

def _softmax(x, axis=-1):
    return jax.nn.softmax(x, axis=axis)

def _gelu(x):
    return jax.nn.gelu(x, approximate=True)

def _silu(x):
    return jax.nn.silu(x)

def _sigmoid(x):
    return jax.nn.sigmoid(x)

def _layernorm(x, axis=-1, eps=1e-05):
    m = jnp.mean(x, axis=axis, keepdims=True)
    v = jnp.var(x, axis=axis, keepdims=True)
    return (x - m) / jnp.sqrt(v + eps)

def _scatter_add(tgt, idx, src, axis=0):
    return tgt.at[idx].add(src)

def _segment_sum(src, seg, n):
    return jax.ops.segment_sum(src, seg, n)
kernel_name = 'mk_xattn_ffn_d2_seqx_r8_90af4d'

def setup_inputs(seed: int=0):
    np.random.seed(seed)
    _w = jnp.asarray

    def _rec_inputs():
        import jax
        import jax.numpy as jnp
        _rk = jax.random.key(seed)
        x = 7.22e-05 + 1 * jax.random.normal(jax.random.fold_in(_rk, 1), (32, 128, 128), jnp.float32)
        _lenS = 128 - jax.random.randint(jax.random.fold_in(_rk, 7), (32,), 0, max(1, 128 // 4) + 1, jnp.int32)
        _lenS2 = 128 - jax.random.randint(jax.random.fold_in(_rk, 8), (32,), 0, max(1, 128 // 4) + 1, jnp.int32)
        _ctx_1024P = jax.random.normal(jax.random.fold_in(_rk, 11), (32, 16, 128), jnp.float32)
        _ctx_1024c = jax.random.dirichlet(jax.random.fold_in(_rk, 511), 0.3 * jnp.ones((16,), jnp.float32), (32, 128))
        _ctx_1024t = jnp.einsum('bsk,bkd->bsd', _ctx_1024c, _ctx_1024P)
        _ctx_1024t = _ctx_1024t * jax.lax.rsqrt(jnp.mean(jnp.square(_ctx_1024t)) + 1e-12) * 0.953939
        ctx_1024 = 4.13588e-05 + 0.999923 * (_ctx_1024t + 0.3 * jax.random.normal(jax.random.fold_in(_rk, 611), (32, 128, 128), jnp.float32))
        _validS = jnp.arange(128)[None, :] < _lenS[:, None]
        _validS2 = jnp.arange(128)[None, :] < _lenS2[:, None]
        _causal = jnp.tril(jnp.ones((128, 128), dtype=bool))
        mask_BxS2_bf1 = jnp.ones((32, 128), dtype=bool)
        return (x, ctx_1024, mask_BxS2_bf1)
    x, ctx_1024, mask_BxS2_bf1 = _rec_inputs()

    def _L0_xattn_setup():
        import jax, jax.numpy as jnp
        import numpy as np
        EMB_DIM = 128
        NUM_HEADS = 16
        HEAD_DIM = EMB_DIM // NUM_HEADS
        key = jax.random.key(seed)
        ks = jax.random.split(key, 7)
        B, S, E = (4, 256, EMB_DIM)
        scale = 1.0 / np.sqrt(E)
        return {'q': jax.random.normal(ks[0], (B, S, E), dtype=jnp.float32), 'k': jax.random.normal(ks[1], (B, S, E), dtype=jnp.float32), 'v': jax.random.normal(ks[2], (B, S, E), dtype=jnp.float32), 'Wq': jax.random.normal(ks[3], (E, E), dtype=jnp.float32) * scale, 'Wk': jax.random.normal(ks[4], (E, E), dtype=jnp.float32) * scale, 'Wv': jax.random.normal(ks[5], (E, E), dtype=jnp.float32) * scale, 'Wo': jax.random.normal(ks[6], (E, E), dtype=jnp.float32) * scale}
    _L0_xattn_all = _L0_xattn_setup()
    _L0_xattn_in = {k: v for k, v in _L0_xattn_all.items() if k in ('Wq', 'Wk', 'Wv', 'Wo')}
    del _L0_xattn_all

    def _L0_ffn_setup():
        import jax, jax.numpy as jnp
        import numpy as np
        import math
        E = 32
        K = 2
        CF = 1.2
        D = 128
        F = 512
        key = jax.random.key(seed)
        ks = jax.random.split(key, 7)
        s = 0.02
        return {'x': jax.random.normal(ks[0], (4, 256, D), jnp.float32), 'gate_w': jax.random.normal(ks[1], (D, E), jnp.float32) * s, 'gate_b': jnp.zeros((E,), jnp.float32), 'w1': jax.random.normal(ks[2], (E, D, F), jnp.float32) * s, 'b1': jnp.zeros((E, F), jnp.float32), 'w2': jax.random.normal(ks[3], (E, F, D), jnp.float32) * s, 'b2': jnp.zeros((E, D), jnp.float32)}
    _L0_ffn_all = _L0_ffn_setup()
    _L0_ffn_in = {k: v for k, v in _L0_ffn_all.items() if k in ('gate_w', 'gate_b', 'w1', 'b1', 'w2', 'b2')}
    del _L0_ffn_all

    def _L1_xattn_setup():
        import jax, jax.numpy as jnp
        import numpy as np
        DIM = 128
        HEADS = 16
        DIM_HEAD = 64
        INNER = HEADS * DIM_HEAD
        EPS = 1e-05

        def layer_norm(x, gamma, beta):
            mu = jnp.mean(x, axis=-1, keepdims=True)
            var = jnp.var(x, axis=-1, keepdims=True)
            return (x - mu) * jax.lax.rsqrt(var + EPS) * gamma + beta
        key = jax.random.key(seed)
        ks = jax.random.split(key, 8)
        b, n, ctx = (2, 256, 256)
        x = jax.random.normal(ks[0], (b, n, DIM), dtype=jnp.float32)
        context = jax.random.normal(ks[1], (b, ctx, DIM), dtype=jnp.float32)
        context_mask = jnp.ones((b, ctx), dtype=bool)
        g1 = jnp.ones((DIM,), jnp.float32)
        b1 = jnp.zeros((DIM,), jnp.float32)
        g2 = jnp.ones((DIM,), jnp.float32)
        b2 = jnp.zeros((DIM,), jnp.float32)
        s = 1.0 / np.sqrt(DIM)
        Wq = jax.random.normal(ks[2], (DIM, INNER), jnp.float32) * s
        Wkv = jax.random.normal(ks[3], (DIM, 2 * INNER), jnp.float32) * s
        Wo = jax.random.normal(ks[4], (INNER, DIM), jnp.float32) * (1.0 / np.sqrt(INNER))
        bo = jnp.zeros((DIM,), jnp.float32)
        return dict(x=x, context=context, context_mask=context_mask, g1=g1, b1=b1, g2=g2, b2=b2, Wq=Wq, Wkv=Wkv, Wo=Wo, bo=bo)
    _L1_xattn_all = _L1_xattn_setup()
    _L1_xattn_in = {k: v for k, v in _L1_xattn_all.items() if k in ('g1', 'b1', 'g2', 'b2', 'Wq', 'Wkv', 'Wo', 'bo')}
    del _L1_xattn_all

    def _L1_ffn_setup():
        import jax, jax.numpy as jnp
        import numpy as np
        TOP_K = 4
        N_GROUP = 4
        TOPK_GROUP = 2
        ROUTED_SCALING = 1.0

        def _route(x_flat, gate_weight, e_bias):
            T = x_flat.shape[0]
            E = gate_weight.shape[0]
            logits = jnp.einsum('th,eh->te', x_flat, gate_weight)
            scores = jax.nn.sigmoid(logits)
            scores_for_choice = scores + e_bias[None, :]
            grp = scores_for_choice.reshape(T, N_GROUP, E // N_GROUP)
            top2, _ = jax.lax.top_k(grp, 2)
            group_scores = top2.sum(axis=-1)
            _, group_idx = jax.lax.top_k(group_scores, TOPK_GROUP)
            group_mask = jax.nn.one_hot(group_idx, N_GROUP, dtype=scores.dtype).sum(axis=1)
            score_mask = jnp.repeat(group_mask, E // N_GROUP, axis=1)
            tmp_scores = jnp.where(score_mask > 0, scores_for_choice, 0.0)
            _, topk_idx = jax.lax.top_k(tmp_scores, TOP_K)
            topk_weight = jnp.take_along_axis(scores, topk_idx, axis=1)
            denom = topk_weight.sum(axis=-1, keepdims=True) + 1e-20
            topk_weight = topk_weight / denom * ROUTED_SCALING
            return (topk_idx, topk_weight)
        key = jax.random.key(seed)
        k1, k2, k3, k4, k5 = jax.random.split(key, 5)
        B, S, H, I, E = (1, 256, 128, 64, 16)
        hidden_states = jax.random.normal(k1, (B, S, H), dtype=jnp.float32)
        gate_weight = jax.random.normal(k2, (E, H), dtype=jnp.float32) * (1.0 / np.sqrt(H))
        e_bias = jnp.zeros((E,), dtype=jnp.float32)
        gate_proj = jax.random.normal(k3, (E, I, H), dtype=jnp.float32) * 0.02
        up_proj = jax.random.normal(k4, (E, I, H), dtype=jnp.float32) * 0.02
        down_proj = jax.random.normal(k5, (E, H, I), dtype=jnp.float32) * 0.02
        return {'hidden_states': hidden_states, 'gate_weight': gate_weight, 'e_bias': e_bias, 'gate_proj': gate_proj, 'up_proj': up_proj, 'down_proj': down_proj}
    _L1_ffn_all = _L1_ffn_setup()
    _L1_ffn_in = {k: v for k, v in _L1_ffn_all.items() if k in ('gate_weight', 'e_bias', 'gate_proj', 'up_proj', 'down_proj')}
    del _L1_ffn_all
    return {'x': x, 'ctx_1024': ctx_1024, 'mask_BxS2_bf1': mask_BxS2_bf1, 'L0_xattn_Wq': _L0_xattn_in['Wq'], 'L0_xattn_Wk': _L0_xattn_in['Wk'], 'L0_xattn_Wv': _L0_xattn_in['Wv'], 'L0_xattn_Wo': _L0_xattn_in['Wo'], 'L0_ffn_gate_w': _L0_ffn_in['gate_w'], 'L0_ffn_gate_b': _L0_ffn_in['gate_b'], 'L0_ffn_w1': _L0_ffn_in['w1'], 'L0_ffn_b1': _L0_ffn_in['b1'], 'L0_ffn_w2': _L0_ffn_in['w2'], 'L0_ffn_b2': _L0_ffn_in['b2'], 'L1_xattn_g1': _L1_xattn_in['g1'], 'L1_xattn_b1': _L1_xattn_in['b1'], 'L1_xattn_g2': _L1_xattn_in['g2'], 'L1_xattn_b2': _L1_xattn_in['b2'], 'L1_xattn_Wq': _L1_xattn_in['Wq'], 'L1_xattn_Wkv': _L1_xattn_in['Wkv'], 'L1_xattn_Wo': _L1_xattn_in['Wo'], 'L1_xattn_bo': _L1_xattn_in['bo'], 'L1_ffn_gate_weight': _L1_ffn_in['gate_weight'], 'L1_ffn_e_bias': _L1_ffn_in['e_bias'], 'L1_ffn_gate_proj': _L1_ffn_in['gate_proj'], 'L1_ffn_up_proj': _L1_ffn_in['up_proj'], 'L1_ffn_down_proj': _L1_ffn_in['down_proj']}

def reference(x, ctx_1024, mask_BxS2_bf1, L0_xattn_Wq, L0_xattn_Wk, L0_xattn_Wv, L0_xattn_Wo, L0_ffn_gate_w, L0_ffn_gate_b, L0_ffn_w1, L0_ffn_b1, L0_ffn_w2, L0_ffn_b2, L1_xattn_g1, L1_xattn_b1, L1_xattn_g2, L1_xattn_b2, L1_xattn_Wq, L1_xattn_Wkv, L1_xattn_Wo, L1_xattn_bo, L1_ffn_gate_weight, L1_ffn_e_bias, L1_ffn_gate_proj, L1_ffn_up_proj, L1_ffn_down_proj):
    import jax
    import jax.numpy as jnp

    def _L0_xattn_ref(q, k, v, Wq, Wk, Wv, Wo):
        import jax, jax.numpy as jnp
        import numpy as np
        EMB_DIM = 128
        NUM_HEADS = 16
        HEAD_DIM = EMB_DIM // NUM_HEADS
        B, S, E = q.shape
        H, D = (NUM_HEADS, HEAD_DIM)
        qh = (q @ Wq.T).reshape(B, S, H, D).transpose(0, 2, 1, 3)
        kh = (k @ Wk.T).reshape(B, S, H, D).transpose(0, 2, 1, 3)
        vh = (v @ Wv.T).reshape(B, S, H, D).transpose(0, 2, 1, 3)
        scores = jnp.einsum('bhse,bhte->bhst', qh, kh) / jnp.sqrt(jnp.float32(D))
        attn = jax.nn.softmax(scores, axis=-1)
        out = jnp.einsum('bhst,bhtd->bshd', attn, vh).reshape(B, S, E)
        return out @ Wo.T

    def _L0_ffn_ref(x, gate_w, gate_b, w1, b1, w2, b2):
        import jax, jax.numpy as jnp
        import numpy as np
        import math
        E = 32
        K = 2
        CF = 1.2
        D = 128
        F = 512
        orig_shape = x.shape
        xt = x.reshape(-1, D)
        T = xt.shape[0]
        C = int(math.ceil(T * K / E * CF))
        logits = xt @ gate_w + gate_b
        probs = jax.nn.softmax(logits, axis=-1)
        top_w, top_i = jax.lax.top_k(probs, K)
        w = top_w / jnp.sum(top_w, axis=-1, keepdims=True)
        flat_e = top_i.reshape(-1)
        oh = jax.nn.one_hot(flat_e, E, dtype=jnp.int32)
        pos_all = jnp.cumsum(oh, axis=0) - 1
        pos = jnp.take_along_axis(pos_all, flat_e[:, None], axis=1)[:, 0]
        valid = pos < C
        pos_d = jnp.where(valid, pos, C)
        x_rep = jnp.repeat(xt, K, axis=0)
        xe = jnp.zeros((E, C, D), x.dtype).at[flat_e, pos_d].add(x_rep, mode='drop')
        he = jax.nn.gelu(jnp.einsum('ecd,edf->ecf', xe, w1) + b1[:, None, :], approximate=False)
        ye = jnp.einsum('ecf,efd->ecd', he, w2) + b2[:, None, :]
        y_flat = ye[flat_e, jnp.minimum(pos, C - 1)] * valid[:, None].astype(x.dtype)
        y = (y_flat.reshape(T, K, D) * w[..., None]).sum(axis=1)
        return y.reshape(orig_shape)

    def _L1_xattn_ref(x, context, context_mask, g1, b1, g2, b2, Wq, Wkv, Wo, bo):
        import jax, jax.numpy as jnp
        import numpy as np
        DIM = 128
        HEADS = 16
        DIM_HEAD = 64
        INNER = HEADS * DIM_HEAD
        EPS = 1e-05

        def layer_norm(x, gamma, beta):
            mu = jnp.mean(x, axis=-1, keepdims=True)
            var = jnp.var(x, axis=-1, keepdims=True)
            return (x - mu) * jax.lax.rsqrt(var + EPS) * gamma + beta
        scale = DIM_HEAD ** (-0.5)
        xn = layer_norm(x, g1, b1)
        cn = layer_norm(context, g2, b2)
        q = xn @ Wq
        kv_x = xn @ Wkv
        kv_c = cn @ Wkv
        k_in, v_in = jnp.split(kv_x, 2, axis=-1)
        k_c, v_c = jnp.split(kv_c, 2, axis=-1)
        k = jnp.concatenate([k_c, k_in], axis=1)
        v = jnp.concatenate([v_c, v_in], axis=1)

        def split_heads(t):
            b_, n_, _ = t.shape
            return t.reshape(b_, n_, HEADS, DIM_HEAD).transpose(0, 2, 1, 3)
        q, k, v = map(split_heads, (q, k, v))
        q = q * scale
        i, j = (q.shape[2], k.shape[2])
        mask_value = -jnp.finfo(q.dtype).max
        sim = jnp.einsum('bhid,bhjd->bhij', q, k)
        cm = jnp.pad(context_mask, ((0, 0), (0, j - context_mask.shape[-1])), constant_values=True)
        sim = jnp.where(cm[:, None, None, :], sim, mask_value)
        causal = jnp.triu(jnp.ones((i, j), dtype=bool), k=j - i + 1)
        sim = jnp.where(causal[None, None], mask_value, sim)
        attn = jax.nn.softmax(sim, axis=-1)
        out = jnp.einsum('bhij,bhjd->bhid', attn, v)
        out = out.transpose(0, 2, 1, 3).reshape(x.shape[0], i, INNER)
        return out @ Wo + bo

    def _L1_ffn_ref(hidden_states, gate_weight, e_bias, gate_proj, up_proj, down_proj):
        import jax, jax.numpy as jnp
        import numpy as np
        TOP_K = 4
        N_GROUP = 4
        TOPK_GROUP = 2
        ROUTED_SCALING = 1.0

        def _route(x_flat, gate_weight, e_bias):
            T = x_flat.shape[0]
            E = gate_weight.shape[0]
            logits = jnp.einsum('th,eh->te', x_flat, gate_weight)
            scores = jax.nn.sigmoid(logits)
            scores_for_choice = scores + e_bias[None, :]
            grp = scores_for_choice.reshape(T, N_GROUP, E // N_GROUP)
            top2, _ = jax.lax.top_k(grp, 2)
            group_scores = top2.sum(axis=-1)
            _, group_idx = jax.lax.top_k(group_scores, TOPK_GROUP)
            group_mask = jax.nn.one_hot(group_idx, N_GROUP, dtype=scores.dtype).sum(axis=1)
            score_mask = jnp.repeat(group_mask, E // N_GROUP, axis=1)
            tmp_scores = jnp.where(score_mask > 0, scores_for_choice, 0.0)
            _, topk_idx = jax.lax.top_k(tmp_scores, TOP_K)
            topk_weight = jnp.take_along_axis(scores, topk_idx, axis=1)
            denom = topk_weight.sum(axis=-1, keepdims=True) + 1e-20
            topk_weight = topk_weight / denom * ROUTED_SCALING
            return (topk_idx, topk_weight)
        B, S, H = hidden_states.shape
        E = gate_proj.shape[0]
        x = hidden_states.reshape(-1, H).astype(jnp.float32)
        topk_idx, topk_weight = _route(x, gate_weight, e_bias)
        combine = (jax.nn.one_hot(topk_idx, E, dtype=x.dtype) * topk_weight[..., None]).sum(axis=1)
        g = jnp.einsum('th,eih->tei', x, gate_proj)
        u = jnp.einsum('th,eih->tei', x, up_proj)
        act = jax.nn.silu(g) * u
        expert_out = jnp.einsum('tei,ehi->teh', act, down_proj)
        y = jnp.einsum('teh,te->th', expert_out, combine)
        return y.reshape(B, S, H)
    x = x + _L0_xattn_ref(_layernorm(x, axis=-1), ctx_1024, ctx_1024, L0_xattn_Wq, L0_xattn_Wk, L0_xattn_Wv, L0_xattn_Wo)
    x = x + _L0_ffn_ref(_layernorm(x, axis=-1), L0_ffn_gate_w, L0_ffn_gate_b, L0_ffn_w1, L0_ffn_b1, L0_ffn_w2, L0_ffn_b2)
    x = x + _L1_xattn_ref(_layernorm(x, axis=-1), ctx_1024, mask_BxS2_bf1, L1_xattn_g1, L1_xattn_b1, L1_xattn_g2, L1_xattn_b2, L1_xattn_Wq, L1_xattn_Wkv, L1_xattn_Wo, L1_xattn_bo)
    x = x + _L1_ffn_ref(_layernorm(x, axis=-1), L1_ffn_gate_weight, L1_ffn_e_bias, L1_ffn_gate_proj, L1_ffn_up_proj, L1_ffn_down_proj)
    return x

_drawn_inputs = setup_inputs


def setup_inputs(seed=0):
    import zlib

    import numpy as np

    out = dict(_drawn_inputs(seed))
    spreads = {'L0_ffn_gate_b': (0.0, 0.1),
     'L0_ffn_b1': (0.0, 0.665),
     'L0_ffn_b2': (0.0, 0.1),
     'L1_xattn_g1': (1.0, 0.2),
     'L1_xattn_b1': (0.0, 0.1),
     'L1_xattn_g2': (1.0, 0.2),
     'L1_xattn_b2': (0.0, 0.1),
     'L1_xattn_bo': (0.0, 0.1),
     'L1_ffn_e_bias': (0.0, 0.8)}
    factors = {'L1_ffn_gate_weight': 8.0,
     'L1_ffn_gate_proj': 8.0,
     'L1_ffn_up_proj': 8.0,
     'L1_ffn_down_proj': 8.0}
    for name, (base, spread) in spreads.items():
        noise = np.random.default_rng([zlib.crc32(name.encode()), seed]).standard_normal(out[name].shape)
        drawn = base * np.exp(spread * noise) if base else spread * noise
        out[name] = jnp.asarray(drawn.astype(out[name].dtype))
    for name, factor in factors.items():
        out[name] = (out[name] * factor).astype(out[name].dtype)
    return out
```

```python
from contextlib import ExitStack

import concourse.bass as bass
from concourse import mybir

F32 = mybir.dt.float32
BF16 = mybir.dt.bfloat16
U32 = mybir.dt.uint32
U8 = mybir.dt.uint8
ALU = mybir.AluOpType
ACT = mybir.ActivationFunctionType
AX_X = mybir.AxisListType.X

P = 128
EPS = 1e-5
MASKED = -1e30

E0, TOPK0, F0 = 32, 2, 512
FC0 = F0 // P
NB0 = 4
SKIP = 16384

H0, D0 = 16, 8
R0 = 4
G0 = H0 // R0

H1, D1 = 16, 64
INNER = H1 * D1
C1 = INNER // P

E1, I1 = 16, 64
EI = E1 * I1


class Links:

    def __init__(self, eng, sem, base):
        self.eng, self.sem, self.base, self.n = eng, sem, base, 0

    def __call__(self, ins):
        self.n += 1
        ins.then_inc(self.sem, 1)
        self.eng.wait_ge(self.sem, self.base + self.n)


class Bearer:

    def __init__(self, tile, columns):
        self.tile, self.columns, self.n = tile, columns, 0

    def __call__(self, eng):
        c = 1 + self.n % self.columns
        self.n += 1
        eng.tensor_tensor(self.tile[0:1, c:c + 1], self.tile[0:1, 0:1], self.tile[0:1, 0:1], ALU.add)


class Shared:
    pass


class Pipe:

    def __init__(self, NT, depth, turn, ahead=0, back=0):
        self.NT, self.depth, self.turn = NT, depth, turn
        self.head = -(-max(depth, ahead, back) // turn) * turn
        self.turns = (NT - ahead - self.head) // turn
        self.last = NT + depth

    def run(self, eng, step):
        for s in range(self.head):
            step(s, s % self.turn)
        if self.turns > 0:
            with eng.Fori(0, self.turns) as t:
                for k in range(self.turn):
                    step(self.turn * t + (self.head + k), k)
        for s in range(self.head + max(self.turns, 0) * self.turn, self.last):
            step(s, s % self.turn)

    def has(self, s, lag):
        return not isinstance(s, int) or 0 <= s - lag < self.NT

    def after(self, s, n):
        return not isinstance(s, int) or s >= n


def capacity(tokens):
    return -(-tokens * TOPK0 * 12 // (E0 * 10))


def load_constants(nc, sh):
    s_ms, s_id, s_ones = sh.sem("const_memset"), sh.sem("const_masks"), sh.sem("const_ones")
    with nc.Block() as block:
        @block.gpsimd
        def _(pool):
            pool.memset(sh.ident[:, :], 0.0).then_inc(s_ms, 1)
            pool.memset(sh.tri[:, :], 1.0).then_inc(s_ms, 1)
            pool.memset(sh.causal[:, :], 0.0).then_inc(s_ms, 1)
            pool.memset(sh.neghalf[:, :], -0.5).then_inc(s_ms, 1)
            pool.memset(sh.eps[:, :], EPS).then_inc(s_ms, 1)
            pool.memset(sh.bears[0][:, :], 0.0).then_inc(s_ms, 1)
            pool.memset(sh.bears[1][:, :], 0.0).then_inc(s_ms, 1)
            pool.memset(sh.kones[:, :], 0.0).then_inc(s_ms, 1)
            pool.iota(sh.iota[:, :], pattern=[[1, E0]], base=0, channel_multiplier=0,
                      allow_small_or_imprecise_dtypes=True).then_inc(s_ms, 1)
            pool.wait_ge(s_ms, 9)
            pool.affine_select(out=sh.ident[:, :], in_=sh.ident[:, :], compare_op=ALU.not_equal, fill=1.0,
                               base=0, pattern=[[-1, P]], channel_multiplier=1).then_inc(s_id, 1)
            pool.affine_select(out=sh.tri[:, :], in_=sh.tri[:, :], compare_op=ALU.is_gt, fill=0.0,
                               base=0, pattern=[[1, P]], channel_multiplier=-1).then_inc(s_id, 1)
            pool.affine_select(out=sh.causal[:, :], in_=sh.causal[:, :], compare_op=ALU.is_ge, fill=MASKED,
                               base=0, pattern=[[-1, P]], channel_multiplier=1).then_inc(s_id, 1)
            pool.wait_ge(s_id, 3)
            for r in range(R0):
                pool.memset(sh.kones[32 * r:32 * r + 1, :], 1.0).then_inc(s_id, 1)

        @block.vector
        def _(dve):
            dve.memset(sh.onesb[:, :], 1.0).then_inc(s_ones, 1)
            dve.wait_ge(s_id, 3 + R0)
            dve.tensor_copy(sh.identb[:, :], sh.ident[:, :]).then_inc(s_ones, 1)


def attention0(nc, sh, w, NT):
    C = sh.C
    pipe = Pipe(NT, 4, 4, ahead=1, back=6)
    has, after = pipe.has, pipe.after
    with ExitStack() as ctx:
        def sb(name, shape, dt=F32):
            return ctx.enter_context(nc.sbuf_tensor(name, shape, dt))

        def sem(name):
            return ctx.enter_context(nc.semaphore(name))

        wq = sb("a_wq", [P, H0, 32])
        wk = sb("a_wk", [P, H0, 32])
        wv = sb("a_wv", [P, P])
        wo = sb("a_wo", [P, P])
        gw = sb("a_gw", [P, E0])
        gb = sb("a_gb", [P, E0])
        zero = sb("a_zero", [P, 11 * P])
        cs = [sb(f"a_ctx{i}", [P, P]) for i in range(2)]
        st = sb("a_stats", [P, 2, 6])
        mv = sb("a_meanvar", [P, 2, 2])
        ve = sb("a_vareps", [P, 2, 1])
        rs = sb("a_rstd", [P, 2, 1])
        xn = [sb(f"a_xn{i}", [P, P]) for i in range(2)]
        xn2 = [sb(f"a_xn2_{i}", [P, P]) for i in range(4)]
        tT = [sb(f"a_tT{i}", [P, 4 * P]) for i in range(2)]
        qS = [sb(f"a_q{i}", [P, G0, P]) for i in range(2)]
        kS = [sb(f"a_k{i}", [P, G0, P]) for i in range(2)]
        qA = sb("a_qaug", [P, G0, P])
        vS = [sb(f"a_v{i}", [P, H0, 32]) for i in range(2)]
        pv = sb("a_pv", [P, 4 * P])
        mP = [sb(f"a_maxpad{i}", [P, G0, P]) for i in range(2)]
        pT = sb("a_probs", [P, R0, G0, P])
        ri = sb("a_rinv", [P, H0, 1])
        o = [sb(f"a_o{i}", [P, H0, D0]) for i in range(2)]
        lg = sb("a_logits", [P, E0])
        m8 = sb("a_top8", [P, 8])
        i8 = sb("a_top8i", [P, 8], U32)
        idf = [sb(f"a_expert{i}", [P, TOPK0]) for i in range(2)]
        oh = [sb(f"a_onehot{i}", [P, TOPK0, E0]) for i in range(2)]
        cnt = [sb(f"a_count{i}", [P, E0], BF16) for i in range(2)]
        cacc = sb("a_countsum", [P, E0], BF16)
        dl = [sb(f"a_dl{i}", [P, 1]) for i in range(2)]
        ew = [sb(f"a_ew{i}", [P, TOPK0]) for i in range(2)]
        pre = sb("a_prefix", [P, E0])
        pp = sb("a_pick", [P, TOPK0, E0])
        pos = sb("a_pos", [P, TOPK0])
        val = sb("a_valid", [P, TOPK0])
        slot = sb("a_slot", [P, TOPK0])
        over = sb("a_over", [P, TOPK0])
        sidx = [sb(f"a_sidx{i}", [P, TOPK0], U32) for i in range(4)]
        den = sb("a_den", [P, 1])
        rden = sb("a_rden", [P, 1])
        wgt = sb("a_wgt", [P, TOPK0])
        ps = sh.ps

        s_w, s_zero, s_init = sem("a_weights"), sem("a_zeroed"), sem("a_init")
        s_zm = sem("a_zero_tile")
        s_ctx = [sem(f"a_ctx_loaded{i}") for i in range(2)]
        s_x = [sem(f"a_x_loaded{i}") for i in range(2)]
        s_xstat, s_rstd, s_xn, s_ln = sem("a_xstat"), sem("a_rstd"), sem("a_xn_ready"), sem("a_ln_links")
        s_x2stat, s_rstd2, s_xn2 = sem("a_x2stat"), sem("a_rstd2"), sem("a_xn2_ready")
        s_pool = sem("a_pool_links")
        s_st0, s_st1 = sem("a_stats_links"), sem("a_stats2_links")
        s_T, s_Tev = sem("a_T_done"), sem("a_T_copied")
        s_q, s_k, s_qev, s_kev = sem("a_q_done"), sem("a_k_done"), sem("a_q_copied"), sem("a_k_copied")
        s_R, s_vev = sem("a_R_done"), sem("a_v_copied")
        s_S1, s_max, s_mT, s_qA, s_S2 = (sem("a_S1_done"), sem("a_max_ready"), sem("a_mT_done"),
                                         sem("a_qaug_ready"), sem("a_S2_done"))
        s_exp, s_PV, s_o, s_ol = sem("a_exp_done"), sem("a_PV_done"), sem("a_o_ready"), sem("a_o_links")
        s_x1, s_vz = sem("a_x1_ready"), sem("a_v_zeroed")
        s_pv, s_back = sem("a_pv_copied"), sem("a_pv_back")
        s_lg, s_rt, s_cnt, s_dl, s_ew = (sem("a_logits_ready"), sem("a_router_links"), sem("a_count_ready"),
                                         sem("a_dl_ready"), sem("a_ew_ready"))
        s_pre, s_sl, s_sidx = sem("a_prefix_ready"), sem("a_slot_links"), sem("a_sidx_ready")
        s_sc = [sem(f"a_scattered{i}") for i in range(4)]

        with nc.Block() as block:
            @block.sync
            def _(sp):
                def load(b, u, first):
                    if not first:
                        sp.wait_ge(s_T, b - 1)
                    sp.dma_start(sh.x[:, b, :], w["x"][b, :, :]).then_inc(s_x[u], 16)
                    sp.dma_start(cs[u][:, :], w["ctx"][b, :, :]).then_inc(s_ctx[u], 16)

                load(0, 0, True)
                sp.wait_ge(s_init, 1)
                sp.dma_start(wq[:, :, 1:1 + D0], w["L0_WqT"].rearrange("i (h d) -> i h d", d=D0)).then_inc(s_w, 16)
                sp.dma_start(wk[:, :, 1:1 + D0], w["L0_WkT"].rearrange("i (h d) -> i h d", d=D0)).then_inc(s_w, 16)
                sp.dma_start(wv[:, :], w["L0_WvT"]).then_inc(s_w, 16)
                sp.dma_start(wo[:, :], w["L0_WoT"]).then_inc(s_w, 16)
                sp.dma_start(gw[:, :], w["L0_gw"]).then_inc(s_w, 16)
                sp.dma_start(gb[:, :], w["L0_gb"].broadcast_to([P, E0])).then_inc(s_w, 16)
                load(1, 1, True)
                with sp.Fori(1, NT // 2) as t:
                    load(2 * t, 0, False)
                    load(2 * t + 1, 1, False)
                for u in range(NB0):
                    load_expert(sp, sh, w, u, u)

            @block.gpsimd
            def _(pool):
                pool.memset(zero[:, :], 0.0).then_inc(s_zm, 1)
                pool.wait_ge(s_zm, 1)
                rows = sh.rows
                xe = sh.xe.rearrange("r d -> (r d)")
                n = 0
                while n < rows:
                    k = min(11, (rows - n) // P)
                    pool.dma_start(xe[n * P:(n + k * P) * P].rearrange("(p c) -> p c", p=P),
                                   zero[:, 0:k * P]).then_inc(s_zero, 16)
                    n += k * P
                zeroed = 16 * -(-rows // (11 * P))

                def norm(b, i, stat, done, links):
                    pool.wait_ge(stat, b + 1)
                    pool.tensor_tensor(ve[:, i, :], mv[:, i, 1:2], sh.eps[:, :], ALU.add).then_inc(links, 1)
                    pool.wait_ge(links, b + 1)
                    pool.tensor_tensor(rs[:, i, :], ve[:, i, :], sh.neghalf[:, :], ALU.pow).then_inc(done, 1)

                norm(0, 0, s_xstat, s_rstd, s_pool)

                def step(s, k):
                    if has(s, -1):
                        norm(s + 1, 0, s_xstat, s_rstd, s_pool)
                    if has(s, 2):
                        norm(s - 2, 1, s_x2stat, s_rstd2, s_ln)
                    if has(s, 4):
                        b = s - 4
                        pool.wait_ge(s_zero, zeroed)
                        pool.wait_ge(s_sidx, b + 1)
                        sh.pool_bear(pool)
                        for j in range(TOPK0):
                            pool.indirect_dma_start(
                                sh.xe, bass.IndirectOffsetOnAxis(ap=sidx[k][:, j:j + 1], axis=0),
                                xn2[k][:, :], None, bounds_check=E0 * C - 1, oob_is_err=False).then_inc(s_sc[k], 16)

                pipe.run(pool, step)
                for k in range(4):
                    pool.wait_ge(s_sc[k], 16 * TOPK0 * NT // 4)

            @block.scalar
            def _(act):
                def step(s, k):
                    u = k % 2
                    lo = 0 if has(s, 0) else 2 * P
                    hi = 4 * P if has(s, 3) else 3 * P if has(s, 2) else 2 * P
                    if lo < hi:
                        act.wait_ge(s_T, s + 1)
                        if after(s, 2):
                            act.wait_ge(s_R, s - 1)
                        act.activation(tT[u][:, lo:hi], ps[:, 6, lo:hi], ACT.Copy).then_inc(s_Tev, 1)
                    if has(s, 0):
                        act.wait_ge(s_q, s + 1)
                        act.activation(qS[u][:, :, :], ps[:, 4, :].rearrange("p (g t) -> p g t", g=G0),
                                       ACT.Copy).then_inc(s_qev, 1)
                        act.wait_ge(s_k, s + 1)
                        act.activation(kS[u][:, :, :], ps[:, 5, :].rearrange("p (g t) -> p g t", g=G0),
                                       ACT.Identity, bias=sh.kones[:, 0:1]).then_inc(s_kev, 1)
                    if has(s, 1):
                        for hf in range(2):
                            act.wait_ge(s_S2, 2 * s - 1 + hf)
                            act.activation(pT[:, 2 * hf:2 * hf + 2, :, :],
                                           ps[:, 2 * hf:2 * hf + 2, :].rearrange("p r (g t) -> p r g t", g=G0),
                                           ACT.Exp, scale=float(D0) ** -0.5).then_inc(s_exp, 1)
                        act.wait_ge(s_PV, s)
                        act.activation(pv[:, :], ps[:, 7, :], ACT.Copy).then_inc(s_pv, 1)
                    if has(s, 3):
                        act.wait_ge(s_dl, s - 2)
                        act.activation(ew[(k + 1) % 2][:, 1:2], dl[(k + 1) % 2][:, :], ACT.Exp).then_inc(s_ew, 1)

                pipe.run(act, step)

            @block.tensor
            def _(pe):
                def scores(lhs, rhs, groups=range(G0), tiles=range(R0)):
                    for g in groups:
                        for r in tiles:
                            rows = slice(32 * r, 32 * r + 32)
                            mm = pe.matmul(ps[:, r, P * g:P * g + P], lhs[rows, g, :], rhs[rows, g, :],
                                           start=True, stop=True)
                    return mm

                def r_read(s):
                    if has(s, 0):
                        pe.wait_ge(s_vev, s + 1)
                    if has(s, 2):
                        pe.wait_ge(s_x1, s - 1)
                    if has(s, 3):
                        pe.wait_ge(s_lg, s - 2)
                    if has(s, 4):
                        pe.wait_ge(s_pre, 2 * (s - 3))

                def transposes(s, k):
                    u = k % 2
                    if has(s, 0):
                        pe.wait_ge(s_xn, s + 1)
                        pe.wait_ge(s_ctx[u], 16 * ((s - u) // 2 + 1))
                        pe.transpose(ps[:, 6, 0:P], xn[u][:, :], sh.ident[:, :])
                        mm = pe.transpose(ps[:, 6, P:2 * P], cs[u][:, :], sh.ident[:, :])
                    if has(s, 2):
                        pe.wait_ge(s_o, s - 1)
                        mm = pe.transpose(ps[:, 6, 2 * P:3 * P], o[u][:, :, :].rearrange("p h d -> p (h d)"),
                                          sh.ident[:, :])
                    if has(s, 3):
                        pe.wait_ge(s_xn2, s - 2)
                        mm = pe.transpose(ps[:, 6, 3 * P:4 * P], xn2[(k - 3) % 4][:, :], sh.ident[:, :])
                    mm.then_inc(s_T, 1)

                pe.wait_ge(s_w, 16 * 6)
                transposes(0, 0)

                def step(s, k):
                    u = k % 2
                    if has(s, 0) or has(s, 3):
                        pe.wait_ge(s_Tev, s + 1)
                    if has(s, 0):
                        for g in range(G0):
                            mm = pe.matmul(ps[:, 4, P * g:P * g + P],
                                           wq[:, R0 * g:R0 * g + R0, :].rearrange("p r c -> p (r c)"),
                                           tT[u][:, 0:P], start=True, stop=True)
                        mm.then_inc(s_q, 1)
                        for g in range(G0):
                            mm = pe.matmul(ps[:, 5, P * g:P * g + P],
                                           wk[:, R0 * g:R0 * g + R0, :].rearrange("p r c -> p (r c)"),
                                           tT[u][:, P:2 * P], start=True, stop=True)
                        mm.then_inc(s_k, 1)
                    v = (k + 1) % 2
                    if has(s, 1):
                        pe.wait_ge(s_max, s)
                        for g in range(G0):
                            mm = pe.transpose(ps[:, 6, P * g:P * g + P], mP[v][:, g, :], sh.ident[:, :])
                        mm.then_inc(s_mT, 1)
                    if has(s, 2):
                        mm = pe.matmul(ps[:, 7, 0:P], tT[u][:, 2 * P:3 * P], wo[:, :], start=True, stop=True)
                    if has(s, 3):
                        mm = pe.matmul(ps[:, 7, P:P + E0], tT[u][:, 3 * P:4 * P], gw[:, :], start=True, stop=True)
                    if has(s, 4):
                        pe.wait_ge(s_cnt, s - 3)
                        pe.matmul(ps[:, 7, P + E0:P + 2 * E0], sh.tri[:, :], cnt[u][:, :], start=True, stop=False)
                        mm = pe.matmul(ps[:, 7, P + E0:P + 2 * E0], sh.onesb[:, :], cacc[:, :],
                                       start=False, stop=True)
                    if has(s, 0):
                        mm = pe.matmul(ps[:, 7, 2 * P:3 * P], tT[u][:, P:2 * P], wv[:, :], start=True, stop=True)
                    mm.then_inc(s_R, 1)
                    if has(s, 1):
                        pe.wait_ge(s_qA, s)
                        for hf in range(2):
                            scores(kS[v], qA, tiles=range(2 * hf, 2 * hf + 2)).then_inc(s_S2, 1)
                        r_read(s)
                        for hf in range(2):
                            pe.wait_ge(s_exp, 2 * s - 1 + hf)
                            for h in range(H0):
                                if h % R0 // 2 == hf:
                                    g, t = h // R0, h % R0
                                    mm = pe.matmul(ps[32 * t:32 * t + 32, 7, P * g:P * g + P], vS[v][:, h, :],
                                                   pT[:, t, g, :], start=True, stop=True)
                        mm.then_inc(s_PV, 1)
                    else:
                        r_read(s)
                    if has(s, 0):
                        pe.wait_ge(s_qev, s + 1)
                        pe.wait_ge(s_kev, s + 1)
                        scores(qS[u], kS[u], groups=range(0, 1))
                    if has(s, 1):
                        pe.wait_ge(s_pv, s)
                        for g in range(G0):
                            mm = pe.transpose(ps[:, 7, P * g:P * g + P], pv[:, P * g:P * g + P], sh.ident[:, :])
                        mm.then_inc(s_back, 1)
                    if has(s, 0):
                        scores(qS[u], kS[u], groups=range(1, 3))
                    if has(s + 1, 0) or has(s + 1, 3):
                        transposes(s + 1, (k + 1) % 4)
                    if has(s, 0):
                        scores(qS[u], kS[u], groups=range(3, G0)).then_inc(s_S1, 1)

                pipe.run(pe, step)

            @block.vector
            def _(dve):
                dve.memset(wq[:, :, :], 0.0)
                dve.memset(wk[:, :, :], 0.0).then_inc(s_init, 1)
                dve.memset(cacc[:, :], 0.0)
                for i in range(2):
                    dve.memset(mP[i][:, :, :], 0.0)
                    dve.memset(vS[i][:, :, :], 0.0).then_inc(s_vz, 1)
                    dve.wait_ge(s_vz, i + 1)
                    dve.memset(vS[i][:, :, D0:D0 + 1], 1.0)
                    dve.memset(ew[i][:, 0:1], 1.0)
                dve.memset(ri[:, :, :], 0.0).then_inc(s_init, 1)
                dve.wait_ge(s_init, 2)

                def stats(src, i, links, b, ready):
                    sh.dve_bear(dve)
                    dve.bn_stats(st[:, i, :], src).then_inc(links, 1)
                    dve.wait_ge(links, b + 1)
                    sh.dve_bear(dve)
                    dve.bn_aggr(mv[:, i, :], st[:, i, :]).then_inc(ready, 1)

                def x_stats(b, u):
                    dve.wait_ge(s_x[u], 16 * ((b - u) // 2 + 1))
                    stats(sh.x[:, b, :], 0, s_st0, b, s_xstat)

                def x_norm(b, u):
                    dve.wait_ge(s_rstd, b + 1)
                    if not isinstance(b, int) or b >= 2:
                        dve.wait_ge(s_T, b - 1)
                    dve.tensor_scalar(xn[u][:, :], sh.x[:, b, :], mv[:, 0, 0:1], rs[:, 0, :],
                                      ALU.subtract, ALU.mult).then_inc(s_xn, 1)

                x_stats(0, 0)
                x_norm(0, 0)
                dve.wait_ge(s_w, 16 * 6)

                def step(s, k):
                    u, v = k % 2, (k + 1) % 2
                    if has(s, -1):
                        x_stats(s + 1, v)
                    if has(s, 1):
                        dve.wait_ge(s_S1, s)
                        dve.tensor_reduce(mP[v][:, :, 0:P:32].rearrange("p g r -> p r g"),
                                          ps[:, 0:R0, :].rearrange("p r (g t) -> p r g t", g=G0),
                                          AX_X, ALU.max, negate=True).then_inc(s_max, 1)
                    if has(s, 1):
                        dve.wait_ge(s_mT, s)
                        dve.wait_ge(s_qev, s)
                        dve.tensor_tensor(qA[:, :, :], qS[v][:, :, :],
                                          ps[:, 6, :].rearrange("p (g t) -> p g t", g=G0), ALU.add).then_inc(s_qA, 1)
                    dve.wait_ge(s_R, s + 1)
                    if has(s, 2):
                        dve.tensor_tensor(sh.x[:, s - 2, :], sh.x[:, s - 2, :], ps[:, 7, 0:P],
                                          ALU.add).then_inc(s_x1, 1)
                    if has(s, 3):
                        dve.tensor_tensor(lg[:, :], ps[:, 7, P:P + E0], gb[:, :], ALU.add).then_inc(s_lg, 1)
                    if has(s, 4):
                        dve.tensor_copy(pre[:, :], ps[:, 7, P + E0:P + 2 * E0]).then_inc(s_pre, 1)
                        dve.tensor_tensor(cacc[:, :], cacc[:, :], cnt[u][:, :], ALU.add).then_inc(s_pre, 1)
                    if has(s, 0):
                        dve.tensor_copy(vS[u][:, :, 0:D0],
                                        ps[:, 7, 2 * P:3 * P].rearrange("p (h d) -> p h d", h=H0)).then_inc(s_vev, 1)
                    if has(s, -1):
                        x_norm(s + 1, v)
                    if has(s, 2):
                        dve.wait_ge(s_x1, s - 1)
                        stats(sh.x[:, s - 2, :], 1, s_st1, s - 2, s_x2stat)
                    if has(s, 3):
                        b = s - 3
                        link = Links(dve, s_rt, 5 * b)
                        dve.wait_ge(s_lg, b + 1)
                        sh.dve_bear(dve)
                        link(dve.max(m8[:, :], lg[:, :]))
                        dve.tensor_tensor(dl[v][:, :], m8[:, 1:2], m8[:, 0:1], ALU.subtract).then_inc(s_dl, 1)
                        link(dve.max_index(i8[:, :], m8[:, :], lg[:, :]))
                        link(dve.tensor_copy(idf[v][:, :], i8[:, 0:TOPK0]))
                        for j in range(TOPK0):
                            link(dve.tensor_scalar(oh[v][:, j, :], sh.iota[:, :], idf[v][:, j:j + 1], None,
                                                   ALU.is_equal))
                        dve.tensor_tensor(cnt[v][:, :], oh[v][:, 0, :], oh[v][:, 1, :], ALU.add).then_inc(s_cnt, 1)
                    if has(s, 2):
                        b = s - 2
                        dve.wait_ge(s_rstd2, b + 1)
                        if not isinstance(s, int) or b >= 4:
                            dve.wait_ge(s_sc[(k + 2) % 4], 32 * ((b - (k + 2) % 4) // 4))
                        dve.tensor_scalar(xn2[(k + 2) % 4][:, :], sh.x[:, b, :], mv[:, 1, 0:1], rs[:, 1, :],
                                          ALU.subtract, ALU.mult).then_inc(s_xn2, 1)
                    if has(s, 4):
                        b = s - 4
                        link = Links(dve, s_sl, 11 * b)
                        dve.wait_ge(s_pre, 2 * (b + 1))
                        link(dve.tensor_tensor(pp[:, :, :], oh[u][:, :, :],
                                               pre[:, :].unsqueeze(1).broadcast_to([P, TOPK0, E0]), ALU.mult))
                        link(dve.tensor_reduce(pos[:, :], pp[:, :, :], AX_X, ALU.add))
                        link(dve.tensor_scalar(val[:, :], pos[:, :], float(C), None, ALU.is_lt))
                        link(dve.tensor_scalar(pos[:, :], pos[:, :], float(C - 1), None, ALU.min))
                        link(dve.scalar_tensor_tensor(out=slot[:, :], in0=idf[u][:, :], scalar=float(C),
                                                      in1=pos[:, :], op0=ALU.mult, op1=ALU.add))
                        link(dve.tensor_copy(sh.gidx[:, b, :], slot[:, :]))
                        link(dve.tensor_scalar(over[:, :], val[:, :], -float(SKIP), float(SKIP), ALU.mult, ALU.add))
                        dve.tensor_tensor(sidx[k][:, :], slot[:, :], over[:, :], ALU.add).then_inc(s_sidx, 1)
                        dve.wait_ge(s_ew, b + 1)
                        link(dve.tensor_scalar(den[:, :], ew[u][:, 1:2], 1.0, None, ALU.add))
                        link(dve.reciprocal(rden[:, :], den[:, :]))
                        link(dve.tensor_scalar(wgt[:, :], ew[u][:, :], rden[:, 0:1], None, ALU.mult))
                        link(dve.tensor_tensor(sh.wgt[:, b, :], wgt[:, :], val[:, :],
                                               ALU.mult))
                    if has(s, 1):
                        dve.wait_ge(s_back, s)
                        rows = ps[:, 7, :].rearrange("p (h d) -> p h d", h=H0)
                        dve.reciprocal(ri[:, :, :], rows[:, :, D0:D0 + 1]).then_inc(s_ol, 1)
                        dve.wait_ge(s_ol, s)
                        dve.tensor_tensor(o[v][:, :, :], rows[:, :, 0:D0], ri[:, :, :].broadcast_to([P, H0, D0]),
                                          ALU.mult).then_inc(s_o, 1)

                pipe.run(dve, step)



def load_expert(sp, sh, w, e, u):
    sp.dma_start(sh.e_w1[u][:, :], w["L0_w1"][e, :, :]).then_inc(sh.s_in[u], 16)
    w2 = w["L0_w2"].rearrange("e (p c) d -> e p c d", c=FC0)
    sp.dma_start(sh.e_w2[u][:, :, :], w2[e, :, :, :]).then_inc(sh.s_in[u], 16)


def experts0(nc, sh, w, NT):
    C = sh.C
    J = next(j for j in range(1, C + 1) if C % j == 0 and C // j <= P)
    CP = C // J
    NB = NB0
    pipe = Pipe(E0, 1, NB, ahead=1, back=3)
    with ExitStack() as ctx:
        def sb(name, shape, dt=F32):
            return ctx.enter_context(nc.sbuf_tensor(name, shape, dt))

        def sem(name):
            return ctx.enter_context(nc.semaphore(name))

        w1, w2, s_in = sh.e_w1, sh.e_w2, sh.s_in
        b1 = sb("e_b1", [P, E0, FC0])
        b2 = sb("e_b2", [P, E0, 1])
        xs = [sb(f"e_x{i}", [CP, J, P]) for i in range(NB)]
        xT = [sb(f"e_xT{i}", [P, C]) for i in range(2)]
        hT = [sb(f"e_hT{i}", [P, FC0, C]) for i in range(2)]
        yT = sb("e_yT", [P, C])
        ys = [sb(f"e_y{i}", [CP, J, P]) for i in range(2)]
        ps = sh.ps
        s_b = sem("e_biases")
        s_T, s_xT, s_h, s_g = sem("e_T_done"), sem("e_xT_ready"), sem("e_h_done"), sem("e_gelu_done")
        s_y, s_yT, s_B, s_ys = sem("e_y_done"), sem("e_yT_ready"), sem("e_back_done"), sem("e_ys_ready")
        s_out = [sem(f"e_stored{i}") for i in range(2)]
        xe = sh.xe[0:E0 * C, :].rearrange("(e p j) d -> e p j d", p=CP, j=J)
        ye = sh.ye[0:E0 * C, :].rearrange("(e p j) d -> e p j d", p=CP, j=J)

        with nc.Block() as block:
            @block.sync
            def _(sp):
                sp.dma_start(b1[:, :, :], w["L0_b1"].rearrange("e (p c) -> p e c", c=FC0)).then_inc(s_b, 16)
                sp.dma_start(b2[:, :, 0], w["L0_b2T"]).then_inc(s_b, 16)

                def load(e, u, first):
                    if not first:
                        sp.wait_ge(s_y, e - NB + 1)
                        load_expert(sp, sh, w, e, u)
                    sp.dma_start(xs[u][:, :, :], xe[e, :, :, :]).then_inc(s_in[u], 16)

                for u in range(NB):
                    load(u, u, True)
                load_attention1_weights(sp, sh, w)
                with sp.Fori(1, E0 // NB) as t:
                    for u in range(NB):
                        load(NB * t + u, u, False)

            @block.tensor
            def _(pe):
                def front(e, u):
                    pe.wait_ge(s_in[u], 48 * ((e - u) // NB + 1))
                    if not isinstance(e, int) or e >= 1:
                        pe.wait_ge(s_xT, e)
                    for j in range(J):
                        mm = pe.transpose(ps[:, 6, CP * j:CP * j + CP], xs[u][:, j, :], sh.ident[0:CP, 0:CP])
                    mm.then_inc(s_T, 1)

                def back(e):
                    pe.wait_ge(s_yT, e + 1)
                    if not isinstance(e, int) or e >= 1:
                        pe.wait_ge(s_ys, e)
                    for j in range(J):
                        mm = pe.transpose(ps[0:CP, 7, P * j:P * j + P], yT[:, CP * j:CP * j + CP], sh.ident[:, :])
                    mm.then_inc(s_B, 1)

                front(0, 0)

                def step(e, k):
                    u = k % 2
                    if pipe.has(e, 0):
                        pe.wait_ge(s_xT, e + 1)
                        for c in range(FC0):
                            if pipe.after(e, 1):
                                pe.wait_ge(s_g, FC0 * (e - 1) + c + 1)
                            pe.matmul(ps[:, c, 0:C], w1[k][:, c:F0:FC0], xT[u][:, :],
                                      start=True, stop=True).then_inc(s_h, 1)
                    if pipe.has(e, 1):
                        back(e - 1)
                    if pipe.has(e, -1):
                        front(e + 1, (k + 1) % NB)
                    if pipe.has(e, 0):
                        if pipe.after(e, 2):
                            pe.wait_ge(s_yT, e - 1)
                        for c in range(FC0):
                            pe.wait_ge(s_g, FC0 * e + c + 1)
                            mm = pe.matmul(ps[:, 4 + u, 0:C], w2[k][:, c, :], hT[u][:, c, :],
                                           start=(c == 0), stop=(c == FC0 - 1))
                        mm.then_inc(s_y, 1)

                pipe.run(pe, step)

            @block.scalar
            def _(act):
                act.wait_ge(s_b, 32)

                def step(e, k):
                    u = k % 2
                    if pipe.has(e, 0):
                        for c in range(FC0):
                            act.wait_ge(s_h, FC0 * e + c + 1)
                            if pipe.after(e, 2) and c == 0:
                                act.wait_ge(s_y, e - 1)
                            act.activation(hT[u][:, c, :], ps[:, c, 0:C], ACT.Gelu,
                                           bias=b1[:, e, c:c + 1]).then_inc(s_g, 1)

                pipe.run(act, step)

            @block.vector
            def _(dve):
                dve.wait_ge(s_b, 32)

                def xt_copy(e, u):
                    dve.wait_ge(s_T, e + 1)
                    if not isinstance(e, int) or e >= 2:
                        dve.wait_ge(s_h, FC0 * (e - 1))
                    dve.tensor_copy(xT[u][:, :], ps[:, 6, 0:C]).then_inc(s_xT, 1)

                xt_copy(0, 0)

                def step(e, k):
                    u, v = k % 2, (k + 1) % 2
                    if pipe.has(e, 1):
                        dve.wait_ge(s_B, e)
                        if pipe.after(e, 3):
                            dve.wait_ge(s_out[v], 16 * ((e - 1 - v) // 2))
                        dve.tensor_copy(ys[v][:, :, :],
                                        ps[0:CP, 7, 0:J * P].rearrange("p (j d) -> p j d", j=J)).then_inc(s_ys, 1)
                    if pipe.has(e, -1):
                        xt_copy(e + 1, v)
                    if pipe.has(e, 0):
                        dve.wait_ge(s_y, e + 1)
                        dve.tensor_scalar(yT[:, :], ps[:, 4 + u, 0:C], b2[:, e, :], None,
                                          ALU.add).then_inc(s_yT, 1)

                pipe.run(dve, step)

            @block.gpsimd
            def _(pool):
                def step(e, k):
                    u, v = k % 2, (k + 1) % 2
                    if pipe.has(e, 1):
                        pool.wait_ge(s_ys, e)
                        pool.dma_start(ye[e - 1, :, :, :], ys[v][:, :, :]).then_inc(s_out[v], 16)

                pipe.run(pool, step)
                for u in range(2):
                    pool.wait_ge(s_out[u], 16 * E0 // 2)


def attention1(nc, sh, w, NT):
    pipe = Pipe(NT, 3, 4, ahead=2)
    NG, GH = 4, 4
    T2 = 2 * P
    NL = 7
    with ExitStack() as ctx:
        def sb(name, shape, dt=F32):
            return ctx.enter_context(nc.sbuf_tensor(name, shape, dt))

        def sem(name):
            return ctx.enter_context(nc.semaphore(name))

        A = sb("c_A", [P, H1, P])
        B = sb("c_B", [P, H1, P])
        gB = sb("c_gamma", [P, 2, P])
        bB = sb("c_beta", [P, 2, P])
        bo = sb("c_bo", [P, P])
        mall = sb("c_mask", [P, NT, P], U8)
        cs = [sb(f"c_ctx{i}", [P, P]) for i in range(2)]
        yg = [sb(f"c_y{i}", [P, TOPK0, P]) for i in range(2)]
        gi = [sb(f"c_gidx{i}", [P, TOPK0], U32) for i in range(2)]
        st = sb("c_stats", [P, 2, 6])
        mv = sb("c_meanvar", [P, 2, 2])
        ve = sb("c_vareps", [P, 2, 1])
        rs = sb("c_rstd", [P, 2, 1])
        xa = sb("c_xa", [P, P])
        nn = [sb(f"c_n{i}", [P, 2, P]) for i in range(2)]
        nR = [sb(f"c_nrow{i}", [P, 2, P]) for i in range(4)]
        nT = [sb(f"c_nT{i}", [P, T2]) for i in range(4)]
        tq = [sb(f"c_t{i}", [P, H1, P]) for i in range(2)]
        mb = [sb(f"c_maskbias{i}", [P, T2], BF16) for i in range(2)]
        nm = [sb(f"c_negmax{i}", [P, GH]) for i in range(2)]
        sm = [sb(f"c_sums{i}", [P, GH]) for i in range(2)]
        ri = [sb(f"c_rinv{i}", [P, GH, 1]) for i in range(2)]
        pr = [sb(f"c_p{i}", [P, GH, T2]) for i in range(2)]
        pT = sb("c_pT", [P, 2, GH, P])
        uT = [sb(f"c_uT{i}", [P, GH, P]) for i in range(2)]
        ps = sh.ps

        s_c = sem("c_constants")
        s_p, s_a, s_b = sem("c_products"), sem("c_A_copied"), sem("c_B_copied")
        s_ctx = [sem(f"c_ctx_loaded{i}") for i in range(2)]
        s_gi = sem("c_gidx_ready")
        s_yg = [sem(f"c_y_gathered{i}") for i in range(2)]
        s_l, s_st, s_rs = sem("c_norm_links"), sem("c_stats_ready"), sem("c_rstd_ready")
        s_nc, s_nx, s_nR = sem("c_ctx_normed"), sem("c_x_normed"), sem("c_nrow_ready")
        s_pl, s_pa = sem("c_rstd_links"), sem("c_affine_links")
        s_mb, s_xb, s_sc = sem("c_maskbias_ready"), sem("c_bias_added"), sem("c_scores_masked")
        s_TX, s_nT = sem("c_TX_done"), sem("c_nT_ready")
        s_t, s_tq = sem("c_t_done"), sem("c_t_ready")
        s_S, s_nm, s_e, s_ri = sem("c_scores_done"), sem("c_negmax_ready"), sem("c_exp_done"), sem("c_rinv_ready")
        s_pn, s_T, s_pT = sem("c_probs_ready"), sem("c_T_done"), sem("c_pT_ready")
        s_U, s_uT, s_O, s_x = sem("c_U_done"), sem("c_uT_ready"), sem("c_O_done"), sem("c_x_ready")

        def ahead(s, j, d):
            return pipe.has(s, 2 if j + d < NG else 1)

        def behind(s, j):
            return pipe.has(s, 2 if j else 3)

        with nc.Block() as block:
            @block.sync
            def _(sp):
                for i, k in ((0, "2"), (1, "1")):
                    sp.dma_start(gB[:, i, :], w["L1_g" + k].broadcast_to([P, P])).then_inc(s_c, 16)
                    sp.dma_start(bB[:, i, :], w["L1_b" + k].broadcast_to([P, P])).then_inc(s_c, 16)
                sp.dma_start(bo[:, :], w["L1_bo"].broadcast_to([P, P])).then_inc(s_c, 16)
                sp.dma_start(mall[:, :, :].rearrange("p b t -> p (b t)"),
                             w["mask"].broadcast_to([P, NT * P])).then_inc(s_c, 16)

                def load(b, u, first):
                    if not first:
                        sp.wait_ge(s_nc, b - 1)
                    sp.dma_start(cs[u][:, :], w["ctx"][b, :, :]).then_inc(s_ctx[u], 16)

                load(0, 0, True)
                load(1, 1, True)
                with sp.Fori(1, NT // 2) as t:
                    load(2 * t, 0, False)
                    load(2 * t + 1, 1, False)

            @block.gpsimd
            def _(pool):
                def gather(b, u):
                    pool.wait_ge(s_gi, b + 1)
                    sh.pool_bear(pool)
                    for j in range(TOPK0):
                        pool.indirect_dma_start(yg[u][:, j, :], None, sh.ye,
                                                bass.IndirectOffsetOnAxis(ap=gi[u][:, j:j + 1], axis=0),
                                                bounds_check=E0 * sh.C - 1, oob_is_err=False).then_inc(s_yg[u], 16)

                def rstd(n, i):
                    pool.wait_ge(s_st, n + 1)
                    pool.tensor_tensor(ve[:, i, :], mv[:, i, 1:2], sh.eps[:, :], ALU.add).then_inc(s_pl, 1)
                    pool.wait_ge(s_pl, n + 1)
                    pool.tensor_tensor(rs[:, i, :], ve[:, i, :], sh.neghalf[:, :], ALU.pow).then_inc(s_rs, 1)

                pool.wait_ge(s_c, 16 * 6)
                gather(0, 0)
                gather(1, 1)

                def step(s, k):
                    new = pipe.has(s, 0)
                    for j in range(NG):
                        if ahead(s, j, 1):
                            n = 4 * (s - 2) + j + 1
                            i = (j + 1) % 2
                            pool.wait_ge(s_ri, n + 1)
                            pool.tensor_tensor(pr[i][:, :, :], pr[i][:, :, :],
                                               ri[i][:, :, :].broadcast_to([P, GH, T2]), ALU.mult).then_inc(s_pn, 1)
                        if j == 0 and new:
                            rstd(3 * s, 0)
                            rstd(3 * s + 1, 1)
                        if j == 1 and new:
                            rstd(3 * s + 2, 0)
                        if j == 2 and new:
                            pool.wait_ge(s_nx, s + 1)
                            pool.tensor_tensor(nn[k % 2][:, :, :], nn[k % 2][:, :, :], gB[:, :, :],
                                               ALU.mult).then_inc(s_pa, 1)
                            pool.wait_ge(s_pa, s + 1)
                            if pipe.after(s, 4):
                                pool.wait_ge(s_U, 4 * (s - 3))
                            pool.tensor_tensor(nR[k][:, :, :], nn[k % 2][:, :, :], bB[:, :, :],
                                               ALU.add).then_inc(s_nR, 1)
                    if pipe.has(s, -2):
                        gather(s + 2, k % 2)

                pipe.run(pool, step)

            @block.tensor
            def _(pe):
                weight_products(pe, sh, s_p)
                pe.wait_ge(s_a, 4)
                pe.wait_ge(s_b, 4)

                def step(s, k):
                    for j in range(NG):
                        n = 4 * (s - 2) + j
                        if pipe.has(s, 2):
                            pe.wait_ge(s_pn, n + 1)
                            for kk in range(2):
                                for h in range(GH):
                                    mm = pe.transpose(ps[:, 4 + kk, P * h:P * h + P],
                                                      pr[j % 2][:, h, P * kk:P * kk + P], sh.ident[:, :])
                            mm.then_inc(s_T, 1)
                        if ahead(s, j, 2):
                            jj = (j + 2) % NG
                            b, kb = (s - 2, (k - 2) % 4) if j < 2 else (s - 1, (k - 1) % 4)
                            pe.wait_ge(s_tq, 4 * b + jj + 1)
                            for r in range(2):
                                bank = 2 * (j % 2) + r
                                for i in range(2):
                                    mm = pe.matmul(ps[:, bank, T2 * i:T2 * i + T2],
                                                   tq[kb % 2][:, GH * jj + 2 * r + i, :], nT[kb][:, :],
                                                   start=True, stop=True)
                            mm.then_inc(s_S, 1)
                        if pipe.has(s, 1 if j else 2) and pipe.after(s, 1):
                            pe.wait_ge(s_tq, 4 * (s - 1) + j)
                        if j == 0 and pipe.has(s, 1):
                            pe.wait_ge(s_nR, s)
                            for i in range(2):
                                mm = pe.transpose(ps[:, 7, P + P * i:2 * P + P * i], nR[(k - 1) % 4][:, i, :],
                                                  sh.ident[:, :])
                            mm.then_inc(s_TX, 1)
                        if behind(s, j):
                            pe.wait_ge(s_uT, n)
                            for h in range(GH):
                                mm = pe.matmul(ps[:, 7, 0:P], uT[(j + 1) % 2][:, h, :],
                                               B[:, (GH * j - GH + h) % H1, :], start=(h == 0), stop=(h == GH - 1))
                            mm.then_inc(s_O, 1)
                        if pipe.has(s, 2):
                            pe.wait_ge(s_pT, n + 1)
                            if not (isinstance(s, int) and n < 1):
                                pe.wait_ge(s_uT, n)
                            for kk in range(2):
                                mm = pe.matmul(ps[:, 6, :].rearrange("p (h t) -> p h t", h=GH),
                                               nR[(k - 2) % 4][:, kk, :], pT[:, kk, :, :],
                                               start=(kk == 0), stop=(kk == 1))
                            mm.then_inc(s_U, 1)
                        if behind(s, j):
                            pe.wait_ge(s_x, n)
                        if pipe.has(s, 1):
                            pe.wait_ge(s_nT, s)
                            for h in range(GH):
                                mm = pe.matmul(ps[:, 7, P * h:P * h + P], A[:, GH * j + h, :],
                                               nT[(k - 1) % 4][:, P:T2], start=True, stop=True)
                            mm.then_inc(s_t, 1)

                pipe.run(pe, step)

            @block.scalar
            def _(act):
                copy_A(act, sh, A, s_p, s_a)

                def step(s, k):
                    for j in range(NG):
                        n = 4 * (s - 2) + j
                        if ahead(s, j, 2):
                            i = j % 2
                            act.wait_ge(s_nm, n + 3)
                            for h in range(GH):
                                act.activation(pr[i][:, h, :], pr[i][:, h, :], ACT.Exp, bias=nm[i][:, h:h + 1],
                                               accum_out=sm[i][:, h:h + 1]).then_inc(s_e, 1)
                        if pipe.has(s, 2):
                            act.wait_ge(s_U, n + 1)
                            act.activation(uT[j % 2][:, :, :], ps[:, 6, :].rearrange("p (h t) -> p h t", h=GH),
                                           ACT.Copy).then_inc(s_uT, 1)
                        if pipe.has(s, 1):
                            act.wait_ge(s_t, 4 * (s - 1) + j + 1)
                            act.activation(tq[(k - 1) % 2][:, GH * j:GH * j + GH, :],
                                           ps[:, 7, :].rearrange("p (h t) -> p h t", h=GH),
                                           ACT.Copy).then_inc(s_tq, 1)

                pipe.run(act, step)

            @block.vector
            def _(dve):
                for i in range(2):
                    dve.tensor_copy(mb[i][:, P:T2], sh.causal[:, :])
                for i in range(2):
                    dve.tensor_copy(gi[i][:, :], sh.gidx[:, i, :]).then_inc(s_gi, 1)
                copy_B(dve, sh, B, s_p, s_b)
                dve.wait_ge(s_c, 16 * 6)

                def stats(src, i, link):
                    sh.dve_bear(dve)
                    link(dve.bn_stats(st[:, i, :], src))
                    sh.dve_bear(dve)
                    dve.bn_aggr(mv[:, i, :], st[:, i, :]).then_inc(s_st, 1)

                def combine(s, u, link):
                    dve.wait_ge(s_yg[u], 16 * TOPK0 * ((s - u) // 2 + 1))
                    link(dve.tensor_scalar(xa[:, :], yg[u][:, 0, :], sh.wgt[:, s, 0:1], None, ALU.mult))
                    link(dve.scalar_tensor_tensor(out=xa[:, :], in0=yg[u][:, 1, :], scalar=sh.wgt[:, s, 1:2],
                                                  in1=xa[:, :], op0=ALU.mult, op1=ALU.add))
                    link(dve.tensor_tensor(sh.x[:, s, :], sh.x[:, s, :], xa[:, :], ALU.add))
                    stats(sh.x[:, s, :], 0, link)
                    dve.wait_ge(s_ctx[u], 16 * ((s - u) // 2 + 1))
                    stats(cs[u][:, :], 1, link)

                def norm(out, src, i):
                    return dve.tensor_scalar(out, src, mv[:, i, 0:1], rs[:, i, :], ALU.subtract, ALU.mult)

                def step(s, k):
                    u, new = k % 2, pipe.has(s, 0)
                    link = Links(dve, s_l, NL * s)
                    for j in range(NG):
                        n = 4 * (s - 2) + j
                        if ahead(s, j, 1):
                            i = (j + 1) % 2
                            dve.wait_ge(s_e, 4 * (n + 2))
                            dve.reciprocal(ri[i][:, :, 0], sm[i][:, :]).then_inc(s_ri, 1)
                        if pipe.has(s, 2):
                            dve.wait_ge(s_T, n + 1)
                            dve.tensor_copy(pT[:, :, :, :],
                                            ps[:, 4:6, :].rearrange("p k (h t) -> p k h t", h=GH)).then_inc(s_pT, 1)
                        if ahead(s, j, 2):
                            i = j % 2
                            b, kb = (s - 2, (k - 2) % 4) if j < 2 else (s - 1, (k - 1) % 4)
                            dve.wait_ge(s_mb, b + 1)
                            dve.wait_ge(s_S, n + 3)
                            dve.tensor_tensor(pr[i][:, :, :],
                                              ps[:, 2 * i:2 * i + 2, :].rearrange("p r (h t) -> p (r h) t", h=2),
                                              mb[kb % 2][:, :].unsqueeze(1).broadcast_to([P, GH, T2]),
                                              ALU.add).then_inc(s_sc, 1)
                        if behind(s, j):
                            dve.wait_ge(s_O, n)
                            b = s - 2 if j else s - 3
                            if isinstance(s, int) and n == 1 or not isinstance(s, int) or n > 1:
                                dve.wait_ge(s_xb, b + 1)
                            if not (isinstance(s, int) and n == 1):
                                dve.wait_ge(s_x, n - 1)
                            dve.tensor_tensor(sh.x[:, b, :], sh.x[:, b, :], ps[:, 7, 0:P], ALU.add).then_inc(s_x, 1)
                        if ahead(s, j, 2):
                            i = j % 2
                            dve.wait_ge(s_sc, n + 3)
                            dve.tensor_reduce(nm[i][:, :], pr[i][:, :, :], AX_X, ALU.max,
                                              negate=True).then_inc(s_nm, 1)
                        if j == 0 and pipe.has(s, 1):
                            dve.wait_ge(s_TX, s)
                            dve.tensor_copy(nT[(k - 1) % 4][:, :], ps[:, 7, P:P + T2]).then_inc(s_nT, 1)
                        if new and j == 0:
                            combine(s, u, link)
                        if new and j == 1:
                            dve.wait_ge(s_rs, 3 * s + 2)
                            link(norm(nn[u][:, 1, :], sh.x[:, s, :], 0))
                            norm(nn[u][:, 0, :], cs[u][:, :], 1).then_inc(s_nc, 1)
                            stats(nn[u][:, 1, :], 0, link)
                        if new and j == 2:
                            dve.wait_ge(s_rs, 3 * s + 3)
                            dve.wait_ge(s_nc, s + 1)
                            norm(nn[u][:, 1, :], nn[u][:, 1, :], 0).then_inc(s_nx, 1)
                            dve.tensor_tensor(sh.x[:, s, :], sh.x[:, s, :], bo[:, :], ALU.add).then_inc(s_xb, 1)
                        if new and j == 3:
                            dve.tensor_scalar(mb[u][:, 0:P], mall[:, s, :], 1.0, -MASKED,
                                              ALU.subtract, ALU.mult).then_inc(s_mb, 1)
                    if pipe.has(s, -2):
                        dve.tensor_copy(gi[u][:, :],
                                        sh.gidx[:, s + 2, :]).then_inc(s_gi, 1)

                pipe.run(dve, step)


def load_attention1_weights(sp, sh, w):
    kvT = w["L1_WkvT"].rearrange("(v c p) i -> v p c i", v=2, p=P)
    for dst, src in zip(sh.w1, (w["L1_WqT"].rearrange("(c p) i -> p c i", p=P), kvT[0], kvT[1],
                                w["L1_Wo"].rearrange("(c p) i -> p c i", p=P))):
        sp.dma_start(dst[:, :, :], src).then_inc(sh.s_w1, 16)


def weight_products(pe, sh, s_p):
    wq, wk, wv, wo = sh.w1
    pe.wait_ge(sh.s_w1, 64)
    for bank in range(8):
        l, r = (wq, wk) if bank < 4 else (wv, wo)
        rows = slice(64 * (bank // 2 % 2), 64 * (bank // 2 % 2) + 64)
        for i in range(4):
            c = 4 * (bank % 2) + i
            mm = pe.matmul(sh.ps[:, bank, P * i:P * i + P], l[rows, c, :], r[rows, c, :], start=True, stop=True)
        mm.then_inc(s_p, 1)


def copy_A(act, sh, A, s_p, s_a):
    heads = A[:, :, :].rearrange("p (g i r) t -> p r g i t", g=2, r=2)
    for bank in range(4):
        act.wait_ge(s_p, bank + 1)
        act.mul(heads[:, bank // 2, bank % 2, :, :], sh.ps[:, bank, :].rearrange("p (i t) -> p i t", i=4),
                float(D1) ** -0.5).then_inc(s_a, 1)


def copy_B(dve, sh, B, s_p, s_b):
    heads = B[:, :, :].rearrange("p (g i r) t -> p r g i t", g=2, r=2)
    for bank in range(4):
        dve.wait_ge(s_p, bank + 5)
        dve.tensor_copy(heads[:, bank // 2, bank % 2, :, :],
                        sh.ps[:, 4 + bank, :].rearrange("p (i t) -> p i t", i=4)).then_inc(s_b, 1)


def ffn1(nc, sh, w, NT, out):
    with ExitStack() as ctx:
        def sb(name, shape, dt=F32):
            return ctx.enter_context(nc.sbuf_tensor(name, shape, dt))

        def sem(name):
            return ctx.enter_context(nc.semaphore(name))

        NQ = NT // 4
        fx = Shared()
        fx.NQ = NQ
        fx.xq = sh.x[:, :, :].rearrange("p (q i) d -> p q i d", i=4)
        fx.gp, fx.up = sb("f_gate", [P, EI]), sb("f_up", [P, EI])
        fx.dp = sb("f_down", [P, EI // P, P])
        fx.xT = sb("f_xT", [P, NQ, 4 * P])
        fx.c3 = sb("f_comb3", [P, NT, 3, E1], BF16)
        fx.sel = sb("f_select", [3 * E1, EI // P, 2, I1], BF16)
        fx.s_w = sem("f_weights")
        ffn1_router(nc, sh, w, NT, fx)
        ffn1_experts(nc, sh, NT, out, fx)


def ffn1_router(nc, sh, w, NT, fx):
    NQ, NG, GE = fx.NQ, 4, E1 // 4
    TOPK, TOPG = 4, 2
    pipe = Pipe(NQ, 2, 2, back=4)
    with ExitStack() as ctx:
        def sb(name, shape, dt=F32):
            return ctx.enter_context(nc.sbuf_tensor(name, shape, dt))

        def sem(name):
            return ctx.enter_context(nc.semaphore(name))

        gw, eb = sb("r_gate", [P, E1]), sb("r_bias", [P, E1])
        st = sb("r_stats", [P, 4, 6])
        mv = [sb(f"r_meanvar{i}", [P, 4, 2]) for i in range(2)]
        ve = sb("r_vareps", [P, 4])
        rs = [sb(f"r_rstd{i}", [P, 4]) for i in range(2)]
        xn = [sb(f"r_xn{i}", [P, 4, P]) for i in range(2)]
        xs = [sb(f"r_xT{i}", [P, 4 * P]) for i in range(2)]
        sc = sb("r_scores", [P, NT, E1])
        sf = sb("r_choice", [P, NT, E1])
        mx = sb("r_pairmax", [P, NT * 2 * NG, 1])
        sm = sb("r_pairsum", [P, NT * 2 * NG, 1])
        sa = sb("r_summax", [P, NT * NG, 1])
        gs = sb("r_groups", [P, NT, 8])
        m8 = sb("r_top8", [P, NT, 8])
        i8 = sb("r_top8i", [P, NT, 8], U32)
        idf = sb("r_index", [P, NT, TOPK])
        gm = sb("r_groupmask", [P, NT, TOPG, NG])
        oh = sb("r_onehot", [P, NT, TOPK, E1])
        den = sb("r_sum", [P, NT])
        c = sb("r_weights", [P, NT, E1])
        rem = sb("r_rest", [P, NT, E1])
        ps = sh.ps

        s_w, s_l, s_pl, s_st, s_rs = (sem("r_gate_loaded"), sem("r_links"), sem("r_rstd_links"),
                                      sem("r_stats_ready"), sem("r_rstd_ready"))
        s_xn, s_T, s_xT, s_xs = sem("r_xn_ready"), sem("r_T_done"), sem("r_xT_ready"), sem("r_xs_ready")
        s_lg, s_e, s_sel, s_r = sem("r_logits_done"), sem("r_exp_done"), sem("r_select_links"), sem("r_route_links")

        with nc.Block() as block:
            @block.sync
            def _(sp):
                sp.dma_start(gw[:, :], w["L1_gwT"]).then_inc(s_w, 16)
                sp.dma_start(eb[:, :], w["L1_eb"].broadcast_to([P, E1])).then_inc(s_w, 16)
                sp.dma_start(fx.gp[:, :], w["L1_gpT"]).then_inc(fx.s_w, 16)
                sp.dma_start(fx.up[:, :], w["L1_upT"]).then_inc(fx.s_w, 16)
                sp.dma_start(fx.dp[:, :, :], w["L1_dpT"].rearrange("(c p) d -> p c d", p=P)).then_inc(fx.s_w, 16)

            @block.gpsimd
            def _(pool):
                def step(q, u):
                    if pipe.has(q, 0):
                        pool.wait_ge(s_st, q + 1)
                        if pipe.after(q, 1):
                            pool.wait_ge(s_rs, q)
                        pool.tensor_tensor(ve[:, :], mv[u][:, :, 1], sh.eps[:, :].broadcast_to([P, 4]), ALU.add).then_inc(s_pl, 1)
                        pool.wait_ge(s_pl, q + 1)
                        pool.tensor_tensor(rs[u][:, :], ve[:, :], sh.neghalf[:, :].broadcast_to([P, 4]),
                                           ALU.pow).then_inc(s_rs, 1)
                    if pipe.has(q, 2):
                        pool.wait_ge(s_xs, q - 1)
                        pool.tensor_copy(fx.xT[:, q - 2, :], xs[u][:, :]).then_inc(s_xT, 1)

                pipe.run(pool, step)
                pool.memset(fx.sel[:, :, :, :], 0.0).then_inc(s_sel, 1)
                for i in range(3):
                    pool.wait_ge(s_sel, i + 1)
                    pool.affine_select(out=fx.sel[:, :, :, :], in_=fx.sel[:, :, :, :], compare_op=ALU.not_equal,
                                       fill=1.0, base=-E1 * i, pattern=[[-2, EI // P], [-1, 2], [0, I1]],
                                       channel_multiplier=1).then_inc(s_sel, 1)

            @block.tensor
            def _(pe):
                pe.wait_ge(s_w, 32)

                def step(q, u):
                    v = (u + 1) % 2
                    if pipe.has(q, 1):
                        pe.wait_ge(s_xn, q)
                        if pipe.after(q, 3):
                            pe.wait_ge(s_xs, q - 2)
                        for i in range(4):
                            mm = pe.transpose(ps[:, v, P * i:P * i + P], xn[v][:, i, :], sh.ident[:, :])
                        mm.then_inc(s_T, 1)
                    if pipe.has(q, 2):
                        pe.wait_ge(s_xs, q - 1)
                        if pipe.after(q, 4):
                            pe.wait_ge(s_e, q - 3)
                        for i in range(4):
                            mm = pe.matmul(ps[:, 2 + u, E1 * i:E1 * i + E1], xs[u][:, P * i:P * i + P], gw[:, :],
                                           start=True, stop=True)
                        mm.then_inc(s_lg, 1)

                pipe.run(pe, step)

            @block.scalar
            def _(act):
                scq = sc[:, :, :].rearrange("p (q i) e -> p q (i e)", i=4)

                def step(q, u):
                    if pipe.has(q, 2):
                        act.wait_ge(s_T, q - 1)
                        if pipe.after(q, 4):
                            act.wait_ge(s_lg, q - 3)
                            act.wait_ge(s_xT, q - 3)
                        act.activation(xs[u][:, :], ps[:, u, :], ACT.Copy).then_inc(s_xs, 1)
                        act.wait_ge(s_lg, q - 1)
                        act.activation(scq[:, q - 2, :], ps[:, 2 + u, 0:4 * E1], ACT.Exp, scale=-1.0).then_inc(s_e, 1)

                pipe.run(act, step)

            @block.vector
            def _(dve):
                dve.memset(gs[:, :, NG:8], MASKED)
                dve.wait_ge(s_w, 32)

                def step(q, u):
                    v = (u + 1) % 2
                    if pipe.has(q, 0):
                        if pipe.after(q, 1):
                            dve.wait_ge(s_st, q)
                            sh.dve_bear(dve)
                        for i in range(4):
                            ins = dve.bn_stats(st[:, i, :], fx.xq[:, q, i, :])
                        ins.then_inc(s_l, 1)
                        dve.wait_ge(s_l, q + 1)
                        sh.dve_bear(dve)
                        for i in range(4):
                            ins = dve.bn_aggr(mv[u][:, i, :], st[:, i, :])
                        ins.then_inc(s_st, 1)
                    if pipe.has(q, 1):
                        dve.wait_ge(s_rs, q)
                        if pipe.after(q, 3):
                            dve.wait_ge(s_T, q - 2)
                        for i in range(4):
                            ins = dve.tensor_scalar(xn[v][:, i, :], fx.xq[:, q - 1, i, :], mv[v][:, i, 0:1],
                                                    rs[v][:, i:i + 1], ALU.subtract, ALU.mult)
                        ins.then_inc(s_xn, 1)

                pipe.run(dve, step)

                link = Links(dve, s_r, 0)
                dve.wait_ge(s_e, NQ)
                link(dve.tensor_scalar(sc[:, :, :], sc[:, :, :], 1.0, None, ALU.add))
                link(dve.reciprocal(sc[:, :, :], sc[:, :, :]))
                link(dve.tensor_tensor(sf[:, :, :], sc[:, :, :], eb[:, :].unsqueeze(1).broadcast_to([P, NT, E1]),
                                       ALU.add))
                pairs = sf[:, :, :].rearrange("p b (g r) -> p (b g) r", r=2)
                dve.tensor_tensor(mx[:, :, :], pairs[:, :, 0:1], pairs[:, :, 1:2], ALU.max)
                link(dve.tensor_tensor(sm[:, :, :], pairs[:, :, 0:1], pairs[:, :, 1:2], ALU.add))
                m2 = mx[:, :, :].rearrange("p (g r) o -> p g (r o)", r=2)
                s2 = sm[:, :, :].rearrange("p (g r) o -> p g (r o)", r=2)
                dve.tensor_tensor(sa[:, :, :], s2[:, :, 0:1], s2[:, :, 1:2], ALU.max)
                link(dve.tensor_tensor(mx[:, 0:NT * NG, :], m2[:, :, 0:1], m2[:, :, 1:2], ALU.add))
                link(dve.tensor_tensor(gs[:, :, 0:NG], sa[:, :, 0].rearrange("p (b g) -> p b g", g=NG),
                                       mx[:, 0:NT * NG, 0].rearrange("p (b g) -> p b g", g=NG), ALU.max))

                def top(values, k):
                    for b in range(NT):
                        ins = dve.max(m8[:, b, :], values[:, b, :])
                    link(ins)
                    for b in range(NT):
                        ins = dve.max_index(i8[:, b, :], m8[:, b, :], values[:, b, :])
                    link(ins)
                    link(dve.tensor_copy(idf[:, :, 0:k], i8[:, :, 0:k]))

                top(gs, TOPG)
                for j in range(TOPG):
                    ins = dve.tensor_tensor(gm[:, :, j, :], sh.iota[:, 0:NG].unsqueeze(1).broadcast_to([P, NT, NG]),
                                            idf[:, :, j:j + 1].broadcast_to([P, NT, NG]), ALU.is_equal)
                link(ins)
                link(dve.tensor_tensor(gm[:, :, 0, :], gm[:, :, 0, :], gm[:, :, 1, :], ALU.add))
                for g in range(NG):
                    ins = dve.tensor_tensor(sf[:, :, GE * g:GE * g + GE], sf[:, :, GE * g:GE * g + GE],
                                            gm[:, :, 0, g:g + 1].broadcast_to([P, NT, GE]), ALU.mult)
                link(ins)
                link(dve.tensor_scalar(sf[:, :, :], sf[:, :, :], 0.0, None, ALU.add))
                top(sf, TOPK)
                for j in range(TOPK):
                    ins = dve.tensor_tensor(oh[:, :, j, :], sh.iota[:, 0:E1].unsqueeze(1).broadcast_to([P, NT, E1]),
                                            idf[:, :, j:j + 1].broadcast_to([P, NT, E1]), ALU.is_equal)
                link(ins)
                link(dve.tensor_tensor(oh[:, :, 0:2, :], oh[:, :, 0:2, :], oh[:, :, 2:4, :], ALU.add))
                link(dve.tensor_tensor(oh[:, :, 0, :], oh[:, :, 0, :], oh[:, :, 1, :], ALU.add))
                link(dve.tensor_tensor(c[:, :, :], sc[:, :, :], oh[:, :, 0, :], ALU.mult))
                link(dve.tensor_reduce(den[:, :], c[:, :, :], AX_X, ALU.add))
                link(dve.tensor_scalar(den[:, :], den[:, :], 1e-20, None, ALU.add))
                link(dve.reciprocal(den[:, :], den[:, :]))
                link(dve.tensor_tensor(c[:, :, :], c[:, :, :], den[:, :].unsqueeze(2).broadcast_to([P, NT, E1]),
                                       ALU.mult))
                link(dve.tensor_copy(fx.c3[:, :, 0, :], c[:, :, :]))
                link(dve.tensor_tensor(rem[:, :, :], c[:, :, :], fx.c3[:, :, 0, :], ALU.subtract))
                link(dve.tensor_copy(fx.c3[:, :, 1, :], rem[:, :, :]))
                link(dve.tensor_tensor(c[:, :, :], rem[:, :, :], fx.c3[:, :, 1, :], ALU.subtract))
                dve.tensor_copy(fx.c3[:, :, 2, :], c[:, :, :])


def ffn1_experts(nc, sh, NT, out, fx):
    NC, NQ = EI // P, fx.NQ
    N = 4 * P
    with ExitStack() as ctx:
        def sb(name, shape, dt=F32):
            return ctx.enter_context(nc.sbuf_tensor(name, shape, dt))

        def sem(name):
            return ctx.enter_context(nc.semaphore(name))

        c3T = sb("f_comb3T", [3 * E1, N], BF16)
        sl = [sb(f"f_silu{i}", [P, N]) for i in range(2)]
        gu = [sb(f"f_gated{i}", [P, N]) for i in range(2)]
        hT = [sb(f"f_hidden{i}", [P, N]) for i in range(2)]
        yT = sb("f_yT", [P, N])
        ps = sh.ps
        s_cT, s_c3, s_g, s_u = sem("f_c3T_done"), sem("f_c3T_copied"), sem("f_g_done"), sem("f_u_done")
        s_sl, s_gu, s_h, s_d = sem("f_silu_ready"), sem("f_gated"), sem("f_hidden_ready"), sem("f_down_done")
        s_yT, s_y = sem("f_yT_copied"), sem("f_y_done")
        s_x, s_out = sem("f_x_ready"), sem("f_stored")

        def run(eng, unit, extra):
            for c in range(NC):
                unit(0, c)
            with eng.Fori(1, NQ) as q:
                for c in range(NC):
                    unit(q, c)
            extra(NQ)

        def after(q, c, n):
            return not isinstance(q, int) or q > 0 or c >= n

        with nc.Block() as block:
            @block.tensor
            def _(pe):
                pe.wait_ge(fx.s_w, 48)

                def down(q, c):
                    n, cc = NC * q + c, (c - 1) % NC
                    pe.wait_ge(s_h, n)
                    if cc == 0 and after(q, 0, 1):
                        pe.wait_ge(s_yT, q)
                    pe.matmul(ps[:, 6, :], fx.dp[:, cc, :], hT[cc % 2][:, :],
                              start=(cc == 0), stop=(cc == NC - 1)).then_inc(s_d, 1)

                def rows(q):
                    pe.wait_ge(s_yT, q)
                    for i in range(4):
                        mm = pe.transpose(ps[:, 7, P * i:P * i + P], yT[:, P * i:P * i + P], sh.ident[:, :])
                    mm.then_inc(s_y, 1)

                def unit(q, c):
                    n, u = NC * q + c, c % 2
                    if c == 0:
                        for i in range(4):
                            mm = pe.matmul(ps[0:3 * E1, 7, P * i:P * i + P],
                                           c3q[:, q, i, :], sh.identb[:, :], start=True, stop=True)
                        mm.then_inc(s_cT, 1)
                    if after(q, c, 2):
                        pe.wait_ge(s_sl, n - 1)
                    pe.matmul(ps[:, u, :], fx.gp[:, P * c:P * c + P], fx.xT[:, q, :],
                              start=True, stop=True).then_inc(s_g, 1)
                    if after(q, c, 2):
                        pe.wait_ge(s_h, n - 1)
                    pe.matmul(ps[:, 2 + u, :], fx.up[:, P * c:P * c + P], fx.xT[:, q, :], start=True, stop=True)
                    if c == 0:
                        pe.wait_ge(s_c3, q + 1)
                    pe.matmul(ps[:, 4 + u, :], fx.sel[:, c, :, :].rearrange("k r i -> k (r i)"), c3T[:, :],
                              start=True, stop=True).then_inc(s_u, 1)
                    if after(q, c, 1):
                        down(q, c)
                    if c == 1 and after(q, 0, 1):
                        rows(q)

                c3q = fx.c3[:, :, :, :].rearrange("p (q i) k e -> p q i (k e)", i=4)
                run(pe, unit, lambda q: (down(q, 0), rows(q)))

            @block.scalar
            def _(act):
                def output(q):
                    act.wait_ge(s_d, NC * q)
                    act.activation(yT[:, :], ps[:, 6, :], ACT.Copy).then_inc(s_yT, 1)

                def unit(q, c):
                    n, u = NC * q + c, c % 2
                    if c == 1 and after(q, 0, 1):
                        output(q)
                    if c == 0:
                        act.wait_ge(s_cT, q + 1)
                        act.activation(c3T[:, :], ps[0:3 * E1, 7, :], ACT.Copy).then_inc(s_c3, 1)
                    act.wait_ge(s_g, n + 1)
                    if after(q, c, 2):
                        act.wait_ge(s_gu, n - 1)
                    act.activation(sl[u][:, :], ps[:, u, :], ACT.Silu).then_inc(s_sl, 1)

                run(act, unit, output)

            @block.vector
            def _(dve):
                def add(q):
                    dve.wait_ge(s_y, q)
                    dve.tensor_tensor(fx.xq[:, q - 1, :, :], fx.xq[:, q - 1, :, :],
                                      ps[:, 7, :].rearrange("p (i d) -> p i d", i=4), ALU.add).then_inc(s_x, 1)

                def unit(q, c):
                    n, u = NC * q + c, c % 2
                    dve.wait_ge(s_sl, n + 1)
                    dve.wait_ge(s_u, n + 1)
                    dve.tensor_tensor(gu[u][:, :], sl[u][:, :], ps[:, 2 + u, :], ALU.mult).then_inc(s_gu, 1)
                    dve.wait_ge(s_gu, n + 1)
                    if after(q, c, 2):
                        dve.wait_ge(s_d, n - 1)
                    dve.tensor_tensor(hT[u][:, :], gu[u][:, :], ps[:, 4 + u, :], ALU.mult).then_inc(s_h, 1)
                    if c == 2 and after(q, 0, 1):
                        add(q)

                run(dve, unit, add)

            @block.sync
            def _(sp):
                outq = out.rearrange("(q i) s d -> q s i d", i=4)
                with sp.Fori(0, NQ) as q:
                    sp.wait_ge(s_x, q + 1)
                    sp.dma_start(outq[q, :, :, :], fx.xq[:, q, :, :]).then_inc(s_out, 16)
                sp.wait_ge(s_out, 16 * NQ)


def model(nc, a, out, NT):
    sh = Shared()
    with ExitStack() as ctx:
        def sb(name, shape, dt=F32):
            return ctx.enter_context(nc.sbuf_tensor(name, shape, dt))

        sh.sem = lambda name: ctx.enter_context(nc.semaphore(name))
        sh.C = capacity(NT * P)
        sh.rows = -(-E0 * sh.C // P) * P
        sh.x = sb("x_res", [P, NT, P])
        sh.ident = sb("ident", [P, P])
        sh.identb = sb("identb", [P, P], BF16)
        sh.tri = sb("tri", [P, P], BF16)
        sh.onesb = sb("onesb", [P, P], BF16)
        sh.causal = sb("causal", [P, P], BF16)
        sh.neghalf = sb("neghalf", [P, 1])
        sh.eps = sb("eps", [P, 1])
        sh.bears = [sb(f"bear{i}", [1, 9]) for i in range(2)]
        sh.dve_bear, sh.pool_bear = Bearer(sh.bears[0], 8), Bearer(sh.bears[1], 8)
        sh.kones = sb("kones", [P, 1])
        sh.iota = sb("iota", [P, E0])
        sh.gidx = sb("gidx", [P, NT, TOPK0], U32)
        sh.wgt = sb("gate_wgt", [P, NT, TOPK0])
        sh.ps = ctx.enter_context(nc.psum_tensor("ps", [P, 8, 512], F32))
        sh.xe = nc.dram_tensor("xe", (sh.rows, P), F32, kind="Internal").ap()
        sh.ye = nc.dram_tensor("ye", (E0 * sh.C, P), F32, kind="Internal").ap()
        sh.e_w1 = [sb(f"e_w1_{i}", [P, F0]) for i in range(NB0)]
        sh.e_w2 = [sb(f"e_w2_{i}", [P, FC0, P]) for i in range(NB0)]
        sh.s_in = [sh.sem(f"e_loaded{i}") for i in range(NB0)]
        load_constants(nc, sh)
        attention0(nc, sh, a, NT)
        with ExitStack() as held:
            sh.w1 = [held.enter_context(nc.sbuf_tensor(f"w_{x}", [P, C1, P], F32)) for x in ("qT", "kT", "vT", "o")]
            sh.s_w1 = sh.sem("w_loaded")
            experts0(nc, sh, a, NT)
            attention1(nc, sh, a, NT)
        ffn1(nc, sh, a, NT, out)


def kernel(**inputs):
    import numpy as _np
    import concourse.bacc as _bacc
    from concourse import mybir as _mybir
    from concourse.bass_utils import run_bass_kernel_spmd as _run

    i = {k: _np.asarray(v) for k, v in inputs.items()}
    E, Ii, H = i["L1_ffn_gate_proj"].shape
    laid = {
        "x": i["x"], "ctx": i["ctx_1024"], "mask": i["mask_BxS2_bf1"].view(_np.uint8).reshape(1, -1),
        "L0_WqT": i["L0_xattn_Wq"].T, "L0_WkT": i["L0_xattn_Wk"].T,
        "L0_WvT": i["L0_xattn_Wv"].T, "L0_WoT": i["L0_xattn_Wo"].T,
        "L0_gw": i["L0_ffn_gate_w"], "L0_gb": i["L0_ffn_gate_b"].reshape(1, -1),
        "L0_w1": i["L0_ffn_w1"], "L0_b1": i["L0_ffn_b1"], "L0_w2": i["L0_ffn_w2"], "L0_b2T": i["L0_ffn_b2"].T,
        "L1_g1": i["L1_xattn_g1"].reshape(1, -1), "L1_b1": i["L1_xattn_b1"].reshape(1, -1),
        "L1_g2": i["L1_xattn_g2"].reshape(1, -1), "L1_b2": i["L1_xattn_b2"].reshape(1, -1),
        "L1_WqT": i["L1_xattn_Wq"].T, "L1_WkvT": i["L1_xattn_Wkv"].T, "L1_Wo": i["L1_xattn_Wo"],
        "L1_bo": i["L1_xattn_bo"].reshape(1, -1),
        "L1_gwT": i["L1_ffn_gate_weight"].T, "L1_eb": i["L1_ffn_e_bias"].reshape(1, -1),
        "L1_gpT": i["L1_ffn_gate_proj"].reshape(E * Ii, H).T, "L1_upT": i["L1_ffn_up_proj"].reshape(E * Ii, H).T,
        "L1_dpT": i["L1_ffn_down_proj"].transpose(0, 2, 1).reshape(E * Ii, H),
    }
    nc = _bacc.Bacc("TRN2", target_bir_lowering=False, num_devices=1)
    arrays, args = {}, {}
    for name, a in laid.items():
        a = _np.ascontiguousarray(a)
        arrays[f"in_{name}"] = a
        args[name] = nc.dram_tensor(f"in_{name}", a.shape, _mybir.dt.from_np(a.dtype), kind="ExternalInput").ap()
    out = nc.dram_tensor("out_0", i["x"].shape, F32, kind="ExternalOutput").ap()
    model(nc, args, out, i["x"].shape[0])
    r = _run(nc, [arrays], core_ids=[0])
    return r.results[0]["out_0"]
```
